# Optimizing a Trainium2 kernel written in Bass

```python
import numpy as np
import jax
import jax.numpy as jnp

def _softmax(x, axis=-1):
    return jax.nn.softmax(x, axis=axis)

def _gelu(x):
    return jax.nn.gelu(x, approximate=True)

def _silu(x):
    return jax.nn.silu(x)

def _sigmoid(x):
    return jax.nn.sigmoid(x)

def _layernorm(x, axis=-1, eps=1e-05):
    m = jnp.mean(x, axis=axis, keepdims=True)
    v = jnp.var(x, axis=axis, keepdims=True)
    return (x - m) / jnp.sqrt(v + eps)

def _scatter_add(tgt, idx, src, axis=0):
    return tgt.at[idx].add(src)

def _segment_sum(src, seg, n):
    return jax.ops.segment_sum(src, seg, n)
kernel_name = 'mk_adj_preln_d2_adj_r2_a4334b'

def setup_inputs(seed: int=0):
    np.random.seed(seed)
    _w = jnp.asarray

    def _rec_inputs():
        import jax
        import jax.numpy as jnp
        _gk = jax.random.key(seed)
        x = -0.0005207 + 1.001 * jax.random.normal(jax.random.fold_in(_gk, 1), (32, 256, 256), jnp.float32)
        _a = jax.random.bernoulli(jax.random.fold_in(_gk, 2), 0.0078125, (32, 256, 256))
        _a = jnp.logical_or(_a, jnp.swapaxes(_a, -1, -2))
        _a = jnp.logical_or(_a, jnp.eye(256, dtype=bool))
        adj = _a
        return (x, adj)
    x, adj = _rec_inputs()

    def _L0_gnn_setup():
        import jax, jax.numpy as jnp
        import numpy as np
        EMB = 256
        HEADS = 8
        HEAD_DIM = 64
        INNER = HEADS * HEAD_DIM
        B, S = (2, 1024)
        SCALE = HEAD_DIM ** (-0.5)
        MIN_SCORE = -1000000000.0
        LN_EPS = 1e-05
        key = jax.random.key(seed)
        ks = jax.random.split(key, 6)
        x = jax.random.normal(ks[0], (B, S, EMB), dtype=jnp.float32)
        graph_mask = jax.random.uniform(ks[1], (B, S, S)) < 0.05
        gamma = jnp.ones((EMB,), jnp.float32)
        beta = jnp.zeros((EMB,), jnp.float32)
        w_qkv = jax.random.normal(ks[2], (3 * INNER, EMB), jnp.float32) * EMB ** (-0.5)
        w_out = jax.random.normal(ks[3], (EMB, INNER), jnp.float32) * INNER ** (-0.5)
        b_out = jnp.zeros((EMB,), jnp.float32)
        return {'x': x, 'graph_mask': graph_mask, 'gamma': gamma, 'beta': beta, 'w_qkv': w_qkv, 'w_out': w_out, 'b_out': b_out}
    _L0_gnn_all = _L0_gnn_setup()
    _L0_gnn_in = {k: v for k, v in _L0_gnn_all.items() if k in ('gamma', 'beta', 'w_qkv', 'w_out', 'b_out')}
    del _L0_gnn_all

    def _L1_gnn_setup():
        import jax, jax.numpy as jnp
        import numpy as np
        QUERY_DIM = 256
        HEADS = 4
        DIM_HEAD = 64
        INNER = HEADS * DIM_HEAD
        B, N = (4, 1024)
        key = jax.random.key(seed)
        ks = jax.random.split(key, 6)
        s = 1.0 / np.sqrt(QUERY_DIM)
        x = jax.random.normal(ks[0], (B, N, QUERY_DIM), dtype=jnp.float32)
        adjacency_mask = jax.random.randint(ks[1], (B, N, N), 0, 2) > 0
        Wq = jax.random.normal(ks[2], (QUERY_DIM, INNER), dtype=jnp.float32) * s
        Wk = jax.random.normal(ks[3], (QUERY_DIM, INNER), dtype=jnp.float32) * s
        Wv = jax.random.normal(ks[4], (QUERY_DIM, INNER), dtype=jnp.float32) * s
        Wo = jax.random.normal(ks[5], (INNER, QUERY_DIM), dtype=jnp.float32) * (1.0 / np.sqrt(INNER))
        bo = jnp.zeros((QUERY_DIM,), dtype=jnp.float32)
        return {'x': x, 'adjacency_mask': adjacency_mask, 'Wq': Wq, 'Wk': Wk, 'Wv': Wv, 'Wo': Wo, 'bo': bo}
    _L1_gnn_all = _L1_gnn_setup()
    _L1_gnn_in = {k: v for k, v in _L1_gnn_all.items() if k in ('Wq', 'Wk', 'Wv', 'Wo', 'bo')}
    del _L1_gnn_all
    return {'x': x, 'adj': adj, 'L0_gnn_gamma': _L0_gnn_in['gamma'], 'L0_gnn_beta': _L0_gnn_in['beta'], 'L0_gnn_w_qkv': _L0_gnn_in['w_qkv'], 'L0_gnn_w_out': _L0_gnn_in['w_out'], 'L0_gnn_b_out': _L0_gnn_in['b_out'], 'L1_gnn_Wq': _L1_gnn_in['Wq'], 'L1_gnn_Wk': _L1_gnn_in['Wk'], 'L1_gnn_Wv': _L1_gnn_in['Wv'], 'L1_gnn_Wo': _L1_gnn_in['Wo'], 'L1_gnn_bo': _L1_gnn_in['bo']}

def reference(x, adj, L0_gnn_gamma, L0_gnn_beta, L0_gnn_w_qkv, L0_gnn_w_out, L0_gnn_b_out, L1_gnn_Wq, L1_gnn_Wk, L1_gnn_Wv, L1_gnn_Wo, L1_gnn_bo):
    import jax
    import jax.numpy as jnp

    def _L0_gnn_ref(x, graph_mask, gamma, beta, w_qkv, w_out, b_out):
        import jax, jax.numpy as jnp
        import numpy as np
        EMB = 256
        HEADS = 8
        HEAD_DIM = 64
        INNER = HEADS * HEAD_DIM
        B, S = (2, 1024)
        SCALE = HEAD_DIM ** (-0.5)
        MIN_SCORE = -1000000000.0
        LN_EPS = 1e-05
        bsz, seq_len, _ = x.shape
        mu = jnp.mean(x, axis=-1, keepdims=True)
        var = jnp.mean(jnp.square(x - mu), axis=-1, keepdims=True)
        h = (x - mu) * jax.lax.rsqrt(var + LN_EPS) * gamma + beta
        qkv = h @ w_qkv.T
        q, k, v = jnp.split(qkv, 3, axis=-1)
        q = q.reshape(bsz, seq_len, HEADS, HEAD_DIM)
        k = k.reshape(bsz, seq_len, HEADS, HEAD_DIM)
        v = v.reshape(bsz, seq_len, HEADS, HEAD_DIM)
        scores = jnp.einsum('bihd,bjhd->bhij', q, k) * SCALE
        eye = jnp.eye(seq_len, dtype=bool)[None]
        mask = graph_mask | eye
        scores = jnp.where(mask[:, None], scores, MIN_SCORE)
        probs = jax.nn.softmax(scores, axis=-1)
        out = jnp.einsum('bhij,bjhd->bihd', probs, v)
        out = out.reshape(bsz, seq_len, INNER)
        return out @ w_out.T + b_out

    def _L1_gnn_ref(x, adjacency_mask, Wq, Wk, Wv, Wo, bo):
        import jax, jax.numpy as jnp
        import numpy as np
        QUERY_DIM = 256
        HEADS = 4
        DIM_HEAD = 64
        INNER = HEADS * DIM_HEAD
        B, N = (4, 1024)
        scale = DIM_HEAD ** (-0.5)

        def split_heads(t):
            b, n, _ = t.shape
            return t.reshape(b, n, HEADS, DIM_HEAD).transpose(0, 2, 1, 3)
        q = split_heads(x @ Wq)
        k = split_heads(x @ Wk)
        v = split_heads(x @ Wv)
        sim = jnp.einsum('bhid,bhjd->bhij', q, k) * scale
        neg = -jnp.finfo(sim.dtype).max
        sim = jnp.where(adjacency_mask[:, None, :, :], sim, neg)
        attn = jax.nn.softmax(sim, axis=-1)
        out = jnp.einsum('bhij,bhjd->bhid', attn, v)
        out = out.transpose(0, 2, 1, 3).reshape(x.shape[0], x.shape[1], INNER)
        return out @ Wo + bo
    h = jnp.maximum(_layernorm(x, axis=-1), 0.0)
    x = x + _L0_gnn_ref(h, adj, L0_gnn_gamma, L0_gnn_beta, L0_gnn_w_qkv, L0_gnn_w_out, L0_gnn_b_out)
    h = jnp.maximum(_layernorm(x, axis=-1), 0.0)
    x = x + _L1_gnn_ref(h, adj, L1_gnn_Wq, L1_gnn_Wk, L1_gnn_Wv, L1_gnn_Wo, L1_gnn_bo)
    return x

_drawn_inputs = setup_inputs


def setup_inputs(seed=0):
    import zlib

    import numpy as np

    out = dict(_drawn_inputs(seed))
    spreads = {'L0_gnn_gamma': (1.0, 0.2),
     'L0_gnn_beta': (0.0, 0.1),
     'L0_gnn_b_out': (0.0, 0.1),
     'L1_gnn_bo': (0.0, 0.1)}
    factors = {}
    for name, (base, spread) in spreads.items():
        noise = np.random.default_rng([zlib.crc32(name.encode()), seed]).standard_normal(out[name].shape)
        drawn = base * np.exp(spread * noise) if base else spread * noise
        out[name] = jnp.asarray(drawn.astype(out[name].dtype))
    for name, factor in factors.items():
        out[name] = (out[name] * factor).astype(out[name].dtype)
    return out
```

```python
from contextlib import ExitStack

import concourse.bass as bass
from concourse import mybir

ALU = mybir.AluOpType
ACT = mybir.ActivationFunctionType
F32 = mybir.dt.float32
F32R = mybir.dt.float32r
BF16 = mybir.dt.bfloat16
U8 = mybir.dt.uint8

P = 128
HEAD = 64
PAIR = 2 * HEAD
EPS = 1e-5
MASKED = -3.0e38
LOWEST = -3.4e38


def graph_attention(nc, x, adj, w0, wo0, w1, wo1, gamma, beta, bias0, bias1, out):
    G, N, D = x.shape
    T = N // P
    K = D // P
    assert T == 2 and K == 2
    INNER0 = w0.shape[1] // 3
    INNER1 = w1.shape[1] // 3
    PAIRS0 = INNER0 // PAIR
    PAIRS1 = INNER1 // PAIR
    STEPS = PAIRS0 + PAIRS1
    SCALE = HEAD ** -0.5
    FIRST_TURN, LAST_TURN = -2, G + 1
    FULL_FIRST, FULL_LAST = 3, G - 4
    LOOPS = (FULL_LAST - FULL_FIRST + 1) // 2

    def exists(g):
        return 0 <= g < G

    def clamp(g):
        return min(max(g, 0), G)

    def step_exists(n, s):
        return exists(n) if s < PAIRS0 else exists(n - 1)

    def pairs_before(n, s):
        return (PAIRS0 * clamp(n) + PAIRS1 * clamp(n - 1) + (min(s, PAIRS0) if exists(n) else 0)
                + (max(s - PAIRS0, 0) if exists(n - 1) else 0))

    JOBS = {
        ("qk0", 0): (1, 1), ("qk0", 1): (0, 1), ("turn1", 0): (2, -1), ("out1", 0): (0, -2),
        ("qk0", 2): (1, 1), ("qk1", 0): (2, -1), ("v1", 0): (1, -1), ("qk0", 3): (0, 1),
        ("qk1", 1): (2, -1), ("v0", 0): (1, 1), ("v0", 1): (0, 1), ("turn0", 0): (2, 2), ("out0", 0): (0, 0),
    }
    EARLY = [[("qk0", 0)], [("turn1", 0), ("out1", 0)], [("qk1", 0)], [("qk0", 3)], [("v0", 0)], [("out0", 0)]]
    LATE = [[("qk0", 1)], [("qk0", 2)], [("v1", 0)], [("qk1", 1)], [("v0", 1), ("turn0", 0)], []]
    assert [j for s in range(STEPS) for j in EARLY[s] + LATE[s]] == list(JOBS)
    BANKS = 3
    SPLIT = ("qk0", "qk1", "turn0", "turn1")

    def job_exists(n, job):
        return exists(n + JOBS[job][1])

    def bank_jobs_before(n, job):
        bank, total = JOBS[job][0], 0
        for other, (b, shift) in JOBS.items():
            if b == bank:
                total += clamp(n + shift)
        for other in JOBS:
            if other == job:
                return total
            if JOBS[other][0] == bank and job_exists(n, other):
                total += 1

    def bank_jobs_through(n, job):
        return bank_jobs_before(n, job) + job_exists(n, job)

    def splits_before(n, job):
        total = sum(clamp(n + shift) for (name, _), (_, shift) in JOBS.items() if name in SPLIT)
        for other in JOBS:
            if other == job:
                return total
            if other[0] in SPLIT and job_exists(n, other):
                total += 1

    class Turn:

        def __init__(self, first, register=None):
            self.first, self.register = first, register

        def graph(self, shift):
            g = self.first + shift
            return g if self.register is None else self.register * 2 + g

        def rows(self, array, shift):
            g = self.first + shift
            return array[g] if self.register is None else array[g:][self.register * 2]

        def has(self, shift):
            return exists(self.first + shift)

    def after(turn, f):
        a = f(turn.first)
        if turn.register is None:
            return a
        assert a > 0
        per_pass = f(turn.first + 2) - a
        for m in range(turn.first, FULL_LAST - 1, 2):
            assert f(m + 2) - f(m) == per_pass
        return turn.register * per_pass + a

    def past(turn, f):
        if turn.register is None and f(turn.first) <= 0:
            return None
        return after(turn, f)

    def graphs(turn, shift):
        return after(turn, lambda n: clamp(n + shift + 1))

    def filled(turn, job):
        return after(turn, lambda n: bank_jobs_before(n, job) + 1)

    def drained(turn, job, later=0):
        return after(turn, lambda n: bank_jobs_through(n - later, job))

    def run(eng, one_turn):
        for n in range(FIRST_TURN, FULL_FIRST):
            one_turn(Turn(n))
        with eng.Fori(0, LOOPS) as i:
            one_turn(Turn(FULL_FIRST, i))
            one_turn(Turn(FULL_FIRST + 1, i))
        for n in range(FULL_LAST + 1, LAST_TURN + 1):
            one_turn(Turn(n))

    x_d = x.rearrange("g (t p) d -> g p t d", p=P)
    adj_d = adj.rearrange("g (t p) m -> g p t m", p=P)
    out_d = out.rearrange("g (t p) d -> g p t d", p=P)

    with ExitStack() as ctx:
        def sb(name, shape, dt=F32):
            return ctx.enter_context(nc.sbuf_tensor(name, shape, dt))

        def bank(name):
            return ctx.enter_context(nc.psum_tensor(name, [P, 512], F32))

        def sem(name):
            return ctx.enter_context(nc.semaphore(name))

        W0, WO0 = 0, K * 3 * INNER0
        W1 = WO0 + PAIRS0 * D
        WO1 = W1 + K * 3 * INNER1
        WEND = WO1 + PAIRS1 * D
        weights = sb("weights", [P, WEND])
        weights_hi = sb("weights_hi", [P, WEND], F32R)
        weights_lo = sb("weights_lo", [P, WEND], F32R)

        def weight_views(tile):
            return (tile[:, W0:WO0].rearrange("p (k c) -> p k c", k=K),
                    tile[:, WO0:W1].rearrange("p (k c) -> p k c", k=PAIRS0),
                    tile[:, W1:WO1].rearrange("p (k c) -> p k c", k=K),
                    tile[:, WO1:WEND].rearrange("p (k c) -> p k c", k=PAIRS1))

        w0_raw, wo0_raw, w1_raw, wo1_raw = weight_views(weights)
        w0_hi, wo0_hi, w1_hi, wo1_hi = weight_views(weights_hi)
        w0_lo, wo0_lo, w1_lo, wo1_lo = weight_views(weights_lo)

        w0_qk, w0_v = slice(0, 2 * INNER0), slice(2 * INNER0, 3 * INNER0)
        W0_QK, W0_V, WO0_ALL, W1_ALL, WO1_ALL = range(5)
        w0_in = w0.rearrange("(k p) c -> p k c", p=P)
        chunks = [
            (w0_raw[:, :, w0_qk], w0_hi[:, :, w0_qk], w0_lo[:, :, w0_qk], w0_in[:, :, w0_qk]),
            (w0_raw[:, :, w0_v], w0_hi[:, :, w0_v], w0_lo[:, :, w0_v], w0_in[:, :, w0_v]),
            (wo0_raw, wo0_hi, wo0_lo, wo0.rearrange("(k p) c -> p k c", p=P)),
            (w1_raw, w1_hi, w1_lo, w1.rearrange("(k p) c -> p k c", p=P)),
            (wo1_raw, wo1_hi, wo1_lo, wo1.rearrange("(k p) c -> p k c", p=P)),
        ]
        SPLIT_AT = {(-1, 0): W0_QK, (-1, 2): W0_V, (0, 1): WO0_ALL, (0, 4): W1_ALL, (1, 4): WO1_ALL}

        identity = sb("identity", [P, P])
        off_diagonal = sb("off_diagonal", [P, T, N], BF16)
        gamma_col = sb("gamma_col", [P, K])
        beta_col = sb("beta_col", [P, K])
        bias0_rows = sb("bias0_rows", [P, T, D])
        bias1_rows = sb("bias1_rows", [P, T, D])
        minus_half = sb("minus_half", [P, T])
        carrier = sb("carrier", [P, STEPS + 3])

        x_in = sb("x_in", [P, T, D])
        relu_x = sb("relu_x", [P, T, D])
        h0 = sb("h0", [P, T, D])
        x_mid = sb("x_mid", [P, T, D])
        h1 = sb("h1", [P, T, D])
        stats = sb("stats", [P, 3, T, 6])
        moments = sb("moments", [P, 3, T, 2])
        eps_term = sb("eps_term", [P, 4, T])
        eps_tile = sb("eps_tile", [P, T])
        ln_scale = sb("ln_scale", [P, 2, T])
        x_again = sb("x_again", [P, T, D])
        residual0 = sb("residual0", [P, T, D])
        residual1 = sb("residual1", [P, T, D])
        y = sb("y", [P, T, D])
        adj0 = sb("adj0", [P, T, N], U8)
        adj1 = sb("adj1", [P, T, N], U8)
        mask_new = sb("mask_new", [P, T, N], BF16)
        mask0 = sb("mask0", [P, T, N], BF16)
        mask1 = sb("mask1", [P, T, N], BF16)

        h0T = sb("h0T", [P, K, N])
        h0T_hi = sb("h0T_hi", [P, 2, K, N], F32R)
        h0T_lo = sb("h0T_lo", [P, 2, K, N], F32R)
        h1T_hi = sb("h1T_hi", [P, K, N], F32R)
        h1T_lo = sb("h1T_lo", [P, K, N], F32R)
        qk0_hi = sb("qk0_hi", [P, 2, PAIRS0, 2 * N], F32R)
        qk0_lo = sb("qk0_lo", [P, 2, PAIRS0, 2 * N], F32R)
        qk1_hi = sb("qk1_hi", [P, PAIRS1, 2 * N], F32R)
        qk1_lo = sb("qk1_lo", [P, PAIRS1, 2 * N], F32R)
        values0 = sb("values0", [P, 2, T, INNER0])
        values1 = sb("values1", [P, T, INNER1])

        masked = sb("masked", [P, 2, 2, T, N])
        maxima = sb("maxima", [P, 2, 2, T])
        shift = sb("shift", [P, 2, 2, T])
        probs = sb("probs", [P, 2, 2, T, N])
        sums = sb("sums", [P, 2, 2, T])
        inverse = sb("inverse", [P, 2, 2, T])
        probsT = sb("probsT", [P, 2, 2, T, N])
        attn0_hi = sb("attn0_hi", [P, PAIRS0, N], F32R)
        attn0_lo = sb("attn0_lo", [P, PAIRS0, N], F32R)
        attn1_hi = sb("attn1_hi", [P, PAIRS1, N], F32R)
        attn1_lo = sb("attn1_lo", [P, PAIRS1, N], F32R)

        scores = [bank("scores_even"), bank("scores_odd")]
        turned = [bank("turned_even"), bank("turned_odd")]
        attended = bank("attended")
        jobs = [bank(f"jobs{b}") for b in range(BANKS)]

        w_loaded = [sem(f"w_loaded{c}") for c in range(len(chunks))]
        gamma_beta_loaded = sem("gamma_beta_loaded")
        bias_loaded = sem("bias_loaded")
        x_loaded = sem("x_loaded")
        x_again_loaded = sem("x_again_loaded")
        adj0_loaded = sem("adj0_loaded")
        adj1_loaded = sem("adj1_loaded")
        y_stored = sem("y_stored")
        cleared = sem("cleared")
        constants = sem("constants")
        w_high = sem("w_high")
        w_low = sem("w_low")
        x_stats = sem("x_stats")
        x_moments = sem("x_moments")
        relu_written = sem("relu_written")
        relu_stats = sem("relu_stats")
        relu_moments = sem("relu_moments")
        eps0_written = sem("eps0_written")
        eps_squared_written = sem("eps_squared_written")
        var0_written = sem("var0_written")
        scale0_written = sem("scale0_written")
        h0_written = sem("h0_written")
        mid_stats = sem("mid_stats")
        mid_moments = sem("mid_moments")
        eps1_written = sem("eps1_written")
        scale1_written = sem("scale1_written")
        h1_written = sem("h1_written")
        residual0_written = sem("residual0_written")
        residual1_written = sem("residual1_written")
        mask_new_written = sem("mask_new_written")
        mask0_written = sem("mask0_written")
        mask1_written = sem("mask1_written")
        h0T_low = sem("h0T_low")
        high_written = sem("high_written")
        job_done = [sem(f"job_done{b}") for b in range(BANKS)]
        job_drained = [sem(f"job_drained{b}") for b in range(BANKS)]
        scores_done = sem("scores_done")
        scores_taken = sem("scores_taken")
        maxima_written = sem("maxima_written")
        shift_written = sem("shift_written")
        exps_written = sem("exps_written")
        inverse_written = sem("inverse_written")
        probs_written = sem("probs_written")
        turned_done = sem("turned_done")
        probsT_written = sem("probsT_written")
        attended_done = sem("attended_done")
        attn_high = sem("attn_high")
        attn_low = sem("attn_low")

        block = ctx.enter_context(nc.Block())

        def step_before(n, s):
            return (n, s - 1) if s else (n - 1, STEPS - 1)

        def has_step(turn, s):
            return step_exists(turn.first, s)

        def has_step_before(turn, s):
            return step_exists(*step_before(turn.first, s))

        @block.sync
        def _(sp):
            def load_weights():
                for chunk, (raw, _, _, source) in enumerate(chunks):
                    sp.dma_start(raw, source).then_inc(w_loaded[chunk], 16)

            def one_turn(turn):
                if turn.has(2):
                    old = past(turn, lambda n: clamp(n + 2))
                    if old is not None:
                        sp.wait_ge(relu_written, old)
                    sp.dma_start(x_in[:, :, :], turn.rows(x_d, 2)).then_inc(x_loaded, 16)
                if turn.first == FIRST_TURN:
                    load_weights()
                if turn.has(0):
                    old = past(turn, lambda n: clamp(n))
                    if old is not None:
                        sp.wait_ge(residual0_written, old)
                    sp.dma_start(x_again[:, :, :], turn.rows(x_d, 0)).then_inc(x_again_loaded, 16)
                if turn.has(-2):
                    sp.wait_ge(job_drained[JOBS["out1", 0][0]], drained(turn, ("out1", 0)))
                    sp.dma_start(turn.rows(out_d, -2), y[:, :, :]).then_inc(y_stored, 16)

            run(sp, one_turn)
            sp.wait_ge(y_stored, 16 * G)

        @block.gpsimd
        def _(pool):
            pool.memset(identity[:, :], 0.0).then_inc(cleared, 1)
            pool.memset(off_diagonal[:, :, :], MASKED).then_inc(cleared, 1)
            pool.memset(minus_half[:, :], -0.5).then_inc(cleared, 1)
            pool.memset(eps_tile[:, :], EPS).then_inc(cleared, 1)
            pool.wait_ge(cleared, 4)
            pool.affine_select(out=identity[:, :], in_=identity[:, :], compare_op=ALU.not_equal, fill=1.0,
                               base=0, pattern=[[-1, P]], channel_multiplier=1).then_inc(constants, 1)
            pool.affine_select(out=off_diagonal[:, :, :], in_=off_diagonal[:, :, :],
                               compare_op=ALU.not_equal, fill=0.0, base=0, pattern=[[P, T], [-1, N]],
                               channel_multiplier=1).then_inc(constants, 1)

            def normalize(turn, s):
                for head in range(2):
                    pool.wait_ge(inverse_written, after(turn, lambda n: 2 * pairs_before(n, s) + head + 1))
                    pair = probs[:, s % 2, head, :, :]
                    pool.tensor_tensor(pair, pair, inverse[:, s % 2, head, :].unsqueeze(2).to_broadcast([P, T, N]),
                                       ALU.mult).then_inc(probs_written, 1)

            def scale1(turn):
                pool.wait_ge(mid_moments, graphs(turn, -1))
                pool.tensor_tensor(eps_term[:, 2, :], moments[:, 2, :, 1], eps_tile[:, :], ALU.add)\
                    .then_inc(eps1_written, 1)
                pool.wait_ge(eps1_written, graphs(turn, -1))
                pool.tensor_tensor(ln_scale[:, 1, :], eps_term[:, 2, :], minus_half[:, :],
                                   ALU.pow).then_inc(scale1_written, 1)

            def scale0(turn):
                pool.wait_ge(x_moments, graphs(turn, 2))
                pool.tensor_tensor(eps_term[:, 0, :], moments[:, 0, :, 1], eps_tile[:, :], ALU.add)\
                    .then_inc(eps0_written, 1)
                pool.wait_ge(eps0_written, graphs(turn, 2))
                pool.tensor_tensor(eps_term[:, 3, :], eps_term[:, 0, :], eps_tile[:, :], ALU.mult)\
                    .then_inc(eps_squared_written, 1)
                pool.wait_ge(eps_squared_written, graphs(turn, 2))
                pool.wait_ge(relu_moments, graphs(turn, 2))
                pool.tensor_tensor(eps_term[:, 1, :], eps_term[:, 3, :], moments[:, 1, :, 1],
                                   ALU.add).then_inc(var0_written, 1)
                pool.wait_ge(var0_written, graphs(turn, 2))
                pool.tensor_tensor(ln_scale[:, 0, :], eps_term[:, 1, :], minus_half[:, :],
                                   ALU.pow).then_inc(scale0_written, 1)

            def one_turn(turn):
                for s in range(STEPS):
                    if s == 0 and turn.has(-1):
                        scale1(turn)
                    if s == 2 and turn.has(-1):
                        old = past(turn, lambda n: bank_jobs_through(n, ("out1", 0)))
                        if old is not None:
                            pool.wait_ge(job_drained[JOBS["out1", 0][0]], old)
                        pool.wait_ge(job_drained[JOBS["out0", 0][0]], drained(turn, ("out0", 0), later=1))
                        pool.tensor_tensor(residual1[:, :, :], x_mid[:, :, :], bias1_rows[:, :, :],
                                           ALU.add).then_inc(residual1_written, 1)
                    if s == 3 and turn.has(0):
                        if turn.first == 0:
                            pool.wait_ge(bias_loaded, 16 * 2)
                        pool.wait_ge(x_again_loaded, 16 * graphs(turn, 0))
                        old = past(turn, lambda n: bank_jobs_through(n - 1, ("out0", 0)))
                        if old is not None:
                            pool.wait_ge(job_drained[JOBS["out0", 0][0]], old)
                        pool.tensor_tensor(residual0[:, :, :], x_again[:, :, :], bias0_rows[:, :, :],
                                           ALU.add).then_inc(residual0_written, 1)
                    if s == 3 and turn.has(2):
                        scale0(turn)
                    if has_step(turn, s):
                        normalize(turn, s)

            run(pool, one_turn)

        @block.scalar
        def _(act):
            act.dma_start(gamma_col[:, :], gamma).then_inc(gamma_beta_loaded, 16)
            act.dma_start(beta_col[:, :], beta).then_inc(gamma_beta_loaded, 16)
            act.dma_start(bias0_rows[:, :, :], bias0.partition_broadcast(P)).then_inc(bias_loaded, 16)
            act.dma_start(bias1_rows[:, :, :], bias1.partition_broadcast(P)).then_inc(bias_loaded, 16)

            def weights_high(chunk):
                raw, hi, _, _ = chunks[chunk]
                act.wait_ge(w_loaded[chunk], 16)
                act.activation(hi, raw, ACT.Copy).then_inc(w_high, 1)

            def exps(turn, s, head):
                act.wait_ge(shift_written, after(turn, lambda n: 2 * pairs_before(n, s) + head + 1))
                old = past(turn, lambda n: 2 * pairs_before(n, s) - 4 + head + 1)
                if old is not None:
                    act.wait_ge(turned_done, old)
                for t in range(T):
                    last = act.activation(probs[:, s % 2, head, t, :], masked[:, s % 2, head, t, :], ACT.Exp,
                                          bias=shift[:, s % 2, head, t:t + 1], scale=SCALE,
                                          accum_out=sums[:, s % 2, head, t:t + 1])
                last.then_inc(exps_written, 1)

            def copy_turned(turn, s):
                k = (s - 1) % 2
                for head in range(2):
                    act.wait_ge(turned_done, after(turn, lambda n: 2 * pairs_before(*step_before(n, s)) + head + 1))
                    act.activation(probsT[:, k, head, :, :], turned[head][:, :].rearrange("p (t n) -> p t n", t=T),
                                   ACT.Copy).then_inc(probsT_written, 1)

            def attended_high(turn, s):
                s = (s - 1) % STEPS
                layer0 = s < PAIRS0
                hi = attn0_hi[:, s, :] if layer0 else attn1_hi[:, s - PAIRS0, :]
                act.wait_ge(attended_done, after(turn, lambda n: pairs_before(*step_before(n, (s + 1) % STEPS)) + 1))
                act.activation(hi, attended[:, 0:N], ACT.Copy).then_inc(attn_high, 1)

            def job(turn, j):
                name, p = j
                b, g_shift = JOBS[j]
                even = (turn.first + g_shift) % 2
                if not turn.has(g_shift):
                    return
                if name == "qk0":
                    act.wait_ge(job_done[b], filled(turn, j))
                    act.activation(qk0_hi[:, even, p, :], jobs[b][:, :], ACT.Copy).then_inc(high_written, 1)
                elif name == "qk1":
                    act.wait_ge(job_done[b], filled(turn, j))
                    act.activation(qk1_hi[:, p, :], jobs[b][:, :], ACT.Copy).then_inc(high_written, 1)
                elif name == "turn1":
                    act.wait_ge(job_done[b], filled(turn, j))
                    act.activation(h1T_hi[:, :, :], jobs[b][:, :].rearrange("p (k n) -> p k n", k=K),
                                   ACT.Relu).then_inc(high_written, 1)
                elif name == "turn0":
                    act.wait_ge(job_drained[b], drained(turn, j))
                    act.activation(h0T_hi[:, even, :, :], h0T[:, :, :], ACT.Copy).then_inc(high_written, 1)
                elif name == "v0":
                    act.wait_ge(job_done[b], filled(turn, j))
                    act.activation(values0[:, even, p, :], jobs[b][:, :], ACT.Copy)\
                       .then_inc(job_drained[b], 1)
                elif name == "v1":
                    act.wait_ge(job_done[b], filled(turn, j))
                    act.activation(values1[:, :, :], jobs[b][:, :].rearrange("p (t c) -> p t c", t=T),
                                   ACT.Copy).then_inc(job_drained[b], 1)

            def one_turn(turn):
                if turn.has(1):
                    old = past(turn, lambda n: clamp(n + 1))
                    if old is not None:
                        act.wait_ge(mask_new_written, old)
                    act.dma_start(adj0[:, :, :], turn.rows(adj_d, 1)).then_inc(adj0_loaded, 16)
                if turn.has(-1):
                    old = past(turn, lambda n: clamp(n - 1))
                    if old is not None:
                        act.wait_ge(mask1_written, old)
                    act.dma_start(adj1[:, :, :], turn.rows(adj_d, -1)).then_inc(adj1_loaded, 16)
                for s in range(STEPS):
                    if (turn.first, s) in SPLIT_AT:
                        weights_high(SPLIT_AT[turn.first, s])
                    if has_step_before(turn, s):
                        copy_turned(turn, s)
                    if has_step(turn, s):
                        exps(turn, s, 0)
                    for j in EARLY[s]:
                        job(turn, j)
                    if has_step(turn, s):
                        exps(turn, s, 1)
                    if has_step_before(turn, s):
                        attended_high(turn, s)
                    for j in LATE[s]:
                        job(turn, j)

            run(act, one_turn)

        @block.vector
        def _(dve):

            def weights_low(chunk):
                raw, hi, lo, _ = chunks[chunk]
                dve.wait_ge(w_high, chunk + 1)
                dve.tensor_tensor(lo, raw, hi.bitcast(F32), ALU.subtract).then_inc(w_low, 1)

            def carry_waits(site):
                dve.memset(carrier[:, site:site + 1], 0.0)

            def take_scores(turn, s):
                mask = mask0 if s < PAIRS0 else mask1
                k = s % 2
                dve.wait_ge(scores_done, after(turn, lambda n: pairs_before(n, s) + 1))
                old = past(turn, lambda n: 2 * pairs_before(n, s) - 2)
                if old is not None:
                    dve.wait_ge(exps_written, old)
                if s == 0:
                    dve.wait_ge(mask0_written, graphs(turn, 0))
                if s == PAIRS0:
                    dve.wait_ge(mask1_written, graphs(turn, -1))

                carry_waits(s)

                def take(head, t):
                    return dve.tensor_tensor_reduce(
                        out=masked[:, k, head, t, :], in0=scores[head][:, t * N:(t + 1) * N],
                        in1=mask[:, t, :], scale=1.0, scalar=LOWEST, op0=ALU.add, op1=ALU.max,
                        accum_out=maxima[:, k, head, t:t + 1])

                def make_shift(head):
                    if head == 0:
                        dve.wait_ge(maxima_written, after(turn, lambda n: pairs_before(n, s) + 1))
                    else:
                        dve.wait_ge(scores_taken, after(turn, lambda n: pairs_before(n, s) + 1))
                    dve.tensor_scalar(shift[:, k, head, :], maxima[:, k, head, :], -SCALE, None, ALU.mult)\
                       .then_inc(shift_written, 1)

                take(0, 0)
                take(0, 1).then_inc(maxima_written, 1)
                take(1, 0)
                make_shift(0)
                take(1, 1).then_inc(scores_taken, 1)
                make_shift(1)

            def invert(turn, s, head):
                k = s % 2
                dve.wait_ge(exps_written, after(turn, lambda n: 2 * pairs_before(n, s) + head + 1))
                old = past(turn, lambda n: 2 * pairs_before(n, s) - 4 + head + 1)
                if old is not None:
                    dve.wait_ge(probs_written, old)
                dve.reciprocal(inverse[:, k, head, :], sums[:, k, head, :]).then_inc(inverse_written, 1)

            def attended_low(turn, s):
                s = (s - 1) % STEPS
                layer0 = s < PAIRS0
                hi = attn0_hi[:, s, :] if layer0 else attn1_hi[:, s - PAIRS0, :]
                lo = attn0_lo[:, s, :] if layer0 else attn1_lo[:, s - PAIRS0, :]
                dve.wait_ge(attn_high, after(turn, lambda n: pairs_before(*step_before(n, (s + 1) % STEPS)) + 1))
                dve.tensor_tensor(lo, attended[:, 0:N], hi.bitcast(F32), ALU.subtract).then_inc(attn_low, 1)

            def find_moments(source, row, stats_done, moments_done, turn, shift):
                for t in range(T):
                    last = dve.bn_stats(stats[:, row, t, :], source[:, t, :])
                last.then_inc(stats_done, 1)
                dve.wait_ge(stats_done, graphs(turn, shift))
                carry_waits(STEPS + row)
                for t in range(T):
                    last = dve.bn_aggr(moments[:, row, t, :], stats[:, row, t, :])
                last.then_inc(moments_done, 1)

            def norm0_x(turn):
                old = past(turn, lambda n: clamp(n + 2))
                if old is not None:
                    dve.wait_ge(scale0_written, old)
                dve.wait_ge(x_loaded, 16 * graphs(turn, 2))
                find_moments(x_in, 0, x_stats, x_moments, turn, 2)
                dve.wait_ge(x_moments, graphs(turn, 2))
                for t in range(T):
                    last = dve.tensor_scalar(relu_x[:, t, :], x_in[:, t, :], moments[:, 0, t, 0:1], 0.0,
                                             ALU.subtract, ALU.max)
                last.then_inc(relu_written, 1)

            def norm0_relu(turn):
                dve.wait_ge(relu_written, graphs(turn, 2))
                find_moments(relu_x, 1, relu_stats, relu_moments, turn, 2)

            def norm0_apply(turn):
                dve.wait_ge(scale0_written, graphs(turn, 2))
                for t in range(T):
                    last = dve.tensor_scalar(h0[:, t, :], relu_x[:, t, :], moments[:, 1, t, 0:1],
                                             ln_scale[:, 0, t:t + 1], ALU.subtract, ALU.mult)
                last.then_inc(h0_written, 1)

            def norm1_moments(turn):
                dve.wait_ge(job_drained[JOBS["out0", 0][0]], drained(turn, ("out0", 0), later=1))
                find_moments(x_mid, 2, mid_stats, mid_moments, turn, -1)

            def norm1_apply(turn):
                dve.wait_ge(scale1_written, graphs(turn, -1))
                for t in range(T):
                    last = dve.tensor_scalar(h1[:, t, :], x_mid[:, t, :], moments[:, 2, t, 0:1],
                                             ln_scale[:, 1, t:t + 1], ALU.subtract, ALU.mult)
                last.then_inc(h1_written, 1)

            def job(turn, j):
                name, p = j
                b, g_shift = JOBS[j]
                even = (turn.first + g_shift) % 2
                if not turn.has(g_shift):
                    return

                if name == "qk0":
                    dve.wait_ge(high_written, after(turn, lambda n: splits_before(n, j) + 1))
                    dve.tensor_tensor(qk0_lo[:, even, p, :], jobs[b][:, :], qk0_hi[:, even, p, :].bitcast(F32),
                                      ALU.subtract).then_inc(job_drained[b], 1)
                elif name == "qk1":
                    dve.wait_ge(high_written, after(turn, lambda n: splits_before(n, j) + 1))
                    dve.tensor_tensor(qk1_lo[:, p, :], jobs[b][:, :], qk1_hi[:, p, :].bitcast(F32),
                                      ALU.subtract).then_inc(job_drained[b], 1)
                elif name == "turn1":
                    dve.wait_ge(high_written, after(turn, lambda n: splits_before(n, j) + 1))
                    dve.scalar_tensor_tensor(out=h1T_lo[:, :, :].rearrange("p k n -> p (k n)"), in0=jobs[b][:, :],
                                             scalar=0.0,
                                             in1=h1T_hi[:, :, :].rearrange("p k n -> p (k n)").bitcast(F32),
                                             op0=ALU.max, op1=ALU.subtract).then_inc(job_drained[b], 1)
                elif name == "turn0":
                    if turn.first == FIRST_TURN:
                        dve.wait_ge(gamma_beta_loaded, 16 * 2)
                    dve.wait_ge(job_done[b], filled(turn, j))
                    for k in range(K):
                        last = dve.tensor_scalar(h0T[:, k, :], jobs[b][:, k * N:(k + 1) * N], gamma_col[:, k:k + 1],
                                                 beta_col[:, k:k + 1], ALU.mult, ALU.add)
                    last.then_inc(job_drained[b], 1)
                elif name == "out0":
                    dve.wait_ge(job_done[b], filled(turn, j))
                    dve.wait_ge(residual0_written, graphs(turn, 0))
                    old = past(turn, lambda n: clamp(n))
                    if old is not None:
                        dve.wait_ge(residual1_written, old)
                    dve.tensor_tensor(x_mid[:, :, :], jobs[b][:, :].rearrange("p (t d) -> p t d", t=T),
                                      residual0[:, :, :], ALU.add).then_inc(job_drained[b], 1)
                elif name == "out1":
                    dve.wait_ge(job_done[b], filled(turn, j))
                    dve.wait_ge(residual1_written, graphs(turn, -2))
                    old = past(turn, lambda n: 16 * clamp(n - 2))
                    if old is not None:
                        dve.wait_ge(y_stored, old)
                    dve.tensor_tensor(y[:, :, :], jobs[b][:, :].rearrange("p (t d) -> p t d", t=T),
                                      residual1[:, :, :], ALU.add).then_inc(job_drained[b], 1)

            def h0_low(turn):
                dve.wait_ge(high_written, after(turn, lambda n: splits_before(n, ("turn0", 0)) + 1))
                even = turn.first % 2
                dve.tensor_tensor(h0T_lo[:, even, :, :], h0T[:, :, :], h0T_hi[:, even, :, :].bitcast(F32),
                                  ALU.subtract).then_inc(h0T_low, 1)

            def make_mask0(turn):
                if turn.first == -1:
                    dve.wait_ge(constants, 2)
                dve.wait_ge(adj0_loaded, 16 * graphs(turn, 1))
                dve.tensor_scalar(mask_new[:, :, :], adj0[:, :, :], -1.0, -MASKED, ALU.add, ALU.mult)\
                   .then_inc(mask_new_written, 1)
                dve.wait_ge(mask_new_written, graphs(turn, 1))
                dve.tensor_tensor(mask0[:, :, :], mask_new[:, :, :], off_diagonal[:, :, :], ALU.max)\
                   .then_inc(mask0_written, 1)

            def make_mask1(turn):
                dve.wait_ge(adj1_loaded, 16 * graphs(turn, -1))
                dve.tensor_scalar(mask1[:, :, :], adj1[:, :, :], -1.0, -MASKED, ALU.add, ALU.mult)\
                   .then_inc(mask1_written, 1)

            def one_turn(turn):
                for s in range(STEPS):
                    if (turn.first, s) in SPLIT_AT:
                        weights_low(SPLIT_AT[turn.first, s])
                    if s == 0 and turn.has(-1):
                        norm1_moments(turn)
                    if s == PAIRS0 and turn.has(1):
                        make_mask0(turn)
                    if s == 2 and turn.has(-1):
                        make_mask1(turn)
                    if has_step(turn, s):
                        take_scores(turn, s)
                    if s == 0 and turn.has(-1):
                        norm1_apply(turn)
                    if s == 1 and turn.has(2):
                        norm0_x(turn)
                    if s == 2 and turn.has(2):
                        norm0_relu(turn)
                    if s == 5 and turn.has(2):
                        h0_low(turn)
                    if has_step(turn, s):
                        invert(turn, s, 0)
                    for j in EARLY[s]:
                        job(turn, j)
                    if has_step(turn, s):
                        invert(turn, s, 1)
                    if has_step_before(turn, s):
                        attended_low(turn, s)
                    if s == 3 and turn.has(2):
                        norm0_apply(turn)
                    for j in LATE[s]:
                        job(turn, j)

            run(dve, one_turn)

        @block.tensor
        def _(pe):
            def score(turn, s):
                if s < PAIRS0:
                    pe.wait_ge(job_drained[JOBS["qk0", s][0]], drained(turn, ("qk0", s), later=1))
                    hi, lo = qk0_hi[:, turn.first % 2, s, :], qk0_lo[:, turn.first % 2, s, :]
                else:
                    pe.wait_ge(job_drained[JOBS["qk1", s - PAIRS0][0]], drained(turn, ("qk1", s - PAIRS0)))
                    hi, lo = qk1_hi[:, s - PAIRS0, :], qk1_lo[:, s - PAIRS0, :]
                old = past(turn, lambda n: pairs_before(n, s))
                if old is not None:
                    pe.wait_ge(scores_taken, old)
                for t in range(T):
                    for c, (q, k) in enumerate(((hi, hi), (hi, lo), (lo, hi))):
                        for head in range(2):
                            rows = slice(HEAD * head, HEAD * (head + 1))
                            last = pe.matmul(scores[head][:, t * N:(t + 1) * N], q[rows, t * P:(t + 1) * P],
                                             k[rows, N:2 * N], start=(c == 0), stop=(c == 2))
                last.then_inc(scores_done, 1)

            def turn_probs(turn, s):
                k = (s - 1) % 2
                for head in range(2):
                    pe.wait_ge(probs_written, after(turn, lambda n: 2 * pairs_before(*step_before(n, s)) + head + 1))
                    old = past(turn, lambda n: 2 * pairs_before(*step_before(n, s)) - 2 + head + 1)
                    if old is not None:
                        pe.wait_ge(probsT_written, old)
                    for t in range(T):
                        for c in range(T):
                            last = pe.transpose(turned[head][:, c * N + t * P:c * N + (t + 1) * P],
                                                probs[:, k, head, t, c * P:(c + 1) * P], identity[:, :])
                    last.then_inc(turned_done, 1)

            def attend(turn, s):
                k, at = (s - 1) % 2, (s - 1) % STEPS
                n_first = turn.first - (s == 0)
                if at == 0:
                    pe.wait_ge(job_drained[JOBS["v0", 0][0]], drained(turn, ("v0", 0), later=1))
                    pe.wait_ge(job_drained[JOBS["v0", 1][0]], drained(turn, ("v0", 1), later=1))
                if at == PAIRS0:
                    pe.wait_ge(job_drained[JOBS["v1", 0][0]], drained(turn, ("v1", 0)))
                old = past(turn, lambda n: pairs_before(*step_before(n, s)))
                if old is not None:
                    pe.wait_ge(attn_low, old)
                pe.wait_ge(probsT_written, after(turn, lambda n: 2 * pairs_before(*step_before(n, s)) + 2))
                for t in range(T):
                    for head in range(2):
                        if at < PAIRS0:
                            c = PAIR * at + HEAD * head
                            v = values0[:, n_first % 2, t, c:c + HEAD]
                        else:
                            c = PAIR * (at - PAIRS0) + HEAD * head
                            v = values1[:, t, c:c + HEAD]
                        last = pe.matmul(attended[HEAD * head:HEAD * (head + 1), 0:N], v,
                                         probsT[:, k, head, t, :], start=(t == 0), stop=(t == T - 1))
                last.then_inc(attended_done, 1)

            def products(out_ap, left, right, chunks):
                (left_hi, left_lo), (right_hi, right_lo) = left, right
                for c in range(chunks):
                    for m, (a, b) in enumerate(((left_hi, right_hi), (left_hi, right_lo), (left_lo, right_hi))):
                        last = pe.matmul(out_ap, a(c), b(c), start=(c == 0 and m == 0),
                                         stop=(c == chunks - 1 and m == 2))
                return last

            def parts(hi, lo, f):
                return (lambda c: f(hi, c)), (lambda c: f(lo, c))

            def job(turn, j):
                name, p = j
                b, g_shift = JOBS[j]
                if not turn.has(g_shift):
                    return
                even = (turn.first + g_shift) % 2
                if name in ("qk0", "v0"):
                    if turn.first == -1:
                        pe.wait_ge(w_low, (W0_QK if name == "qk0" else W0_V) + 1)
                    pe.wait_ge(h0T_low, graphs(turn, 1))
                elif name in ("qk1", "v1"):
                    if turn.first == 1:
                        pe.wait_ge(w_low, W1_ALL + 1)
                    pe.wait_ge(job_drained[JOBS["turn1", 0][0]], drained(turn, ("turn1", 0)))
                elif name == "turn0":
                    pe.wait_ge(h0_written, graphs(turn, 2))
                elif name == "turn1":
                    pe.wait_ge(h1_written, graphs(turn, -1))
                elif name == "out0":
                    if turn.first == 0:
                        pe.wait_ge(w_low, WO0_ALL + 1)
                    pe.wait_ge(attn_low, after(turn, lambda n: pairs_before(n, PAIRS0)))
                else:
                    if turn.first == 2:
                        pe.wait_ge(w_low, WO1_ALL + 1)
                    pe.wait_ge(attn_low, after(turn, lambda n: pairs_before(n, 0)))
                old = past(turn, lambda n: bank_jobs_before(n, j))
                if old is not None:
                    pe.wait_ge(job_drained[b], old)
                if name == "qk0":
                    h = parts(h0T_hi, h0T_lo, lambda a, c: a[:, even, c, :])
                    for half in range(2):
                        at = half * INNER0 + p * PAIR
                        last = products(jobs[b][:, half * N:(half + 1) * N],
                                        parts(w0_hi, w0_lo, lambda a, c: a[:, c, at:at + PAIR]), h, K)
                elif name == "qk1":
                    h = parts(h1T_hi, h1T_lo, lambda a, c: a[:, c, :])
                    for half in range(2):
                        at = half * INNER1 + p * PAIR
                        last = products(jobs[b][:, half * N:(half + 1) * N],
                                        parts(w1_hi, w1_lo, lambda a, c: a[:, c, at:at + PAIR]), h, K)
                elif name == "v0":
                    last = products(jobs[b][:, 0:INNER0],
                                    parts(h0T_hi, h0T_lo, lambda a, c: a[:, even, c, p * P:(p + 1) * P]),
                                    parts(w0_hi, w0_lo, lambda a, c: a[:, c, 2 * INNER0:3 * INNER0]), K)
                elif name == "v1":
                    for t in range(T):
                        last = products(jobs[b][:, t * INNER1:(t + 1) * INNER1],
                                        parts(h1T_hi, h1T_lo, lambda a, c: a[:, c, t * P:(t + 1) * P]),
                                        parts(w1_hi, w1_lo, lambda a, c: a[:, c, 2 * INNER1:3 * INNER1]), K)
                elif name == "out0":
                    for t in range(T):
                        last = products(jobs[b][:, t * D:(t + 1) * D],
                                        parts(attn0_hi, attn0_lo, lambda a, c: a[:, c, t * P:(t + 1) * P]),
                                        parts(wo0_hi, wo0_lo, lambda a, c: a[:, c, :]), PAIRS0)
                elif name == "out1":
                    for t in range(T):
                        last = products(jobs[b][:, t * D:(t + 1) * D],
                                        parts(attn1_hi, attn1_lo, lambda a, c: a[:, c, t * P:(t + 1) * P]),
                                        parts(wo1_hi, wo1_lo, lambda a, c: a[:, c, :]), PAIRS1)
                else:
                    h = h0 if name == "turn0" else h1
                    for t in range(T):
                        for k in range(K):
                            last = pe.transpose(jobs[b][:, k * N + t * P:k * N + (t + 1) * P],
                                                h[:, t, k * P:(k + 1) * P], identity[:, :])
                last.then_inc(job_done[b], 1)

            def one_turn(turn):
                for s in range(STEPS):
                    if has_step(turn, s):
                        score(turn, s)
                    if has_step_before(turn, s):
                        turn_probs(turn, s)
                    for j in EARLY[s]:
                        job(turn, j)
                    if has_step_before(turn, s):
                        attend(turn, s)
                    for j in LATE[s]:
                        job(turn, j)

            pe.wait_ge(constants, 1)
            run(pe, one_turn)


def kernel(x, adj, L0_gnn_gamma, L0_gnn_beta, L0_gnn_w_qkv, L0_gnn_w_out, L0_gnn_b_out,
           L1_gnn_Wq, L1_gnn_Wk, L1_gnn_Wv, L1_gnn_Wo, L1_gnn_bo):
    import numpy as np
    import concourse.bacc as bacc
    from concourse.bass_utils import run_bass_kernel_spmd

    x = np.ascontiguousarray(x)
    D = x.shape[-1]
    arrays = {
        "x": x,
        "adj": np.ascontiguousarray(adj),
        "w0": np.ascontiguousarray(np.asarray(L0_gnn_w_qkv).T),
        "wo0": np.ascontiguousarray(np.asarray(L0_gnn_w_out).T),
        "w1": np.ascontiguousarray(np.concatenate([L1_gnn_Wq, L1_gnn_Wk, L1_gnn_Wv], axis=1)),
        "wo1": np.ascontiguousarray(L1_gnn_Wo),
        "gamma": np.ascontiguousarray(np.asarray(L0_gnn_gamma).reshape(D // P, P).T),
        "beta": np.ascontiguousarray(np.asarray(L0_gnn_beta).reshape(D // P, P).T),
        "bias0": np.ascontiguousarray(np.tile(np.asarray(L0_gnn_b_out), (x.shape[1] // P, 1))),
        "bias1": np.ascontiguousarray(np.tile(np.asarray(L1_gnn_bo), (x.shape[1] // P, 1))),
    }
    nc = bacc.Bacc("TRN2", target_bir_lowering=False, num_devices=1)
    args = [nc.dram_tensor(f"in_{name}", a.shape, mybir.dt.from_np(a.dtype), kind="ExternalInput").ap()
            for name, a in arrays.items()]
    args.append(nc.dram_tensor("out_x", x.shape, F32, kind="ExternalOutput").ap())
    graph_attention(nc, *args)
    result = run_bass_kernel_spmd(nc, [{f"in_{name}": a for name, a in arrays.items()}], core_ids=[0])
    return result.results[0]["out_x"]
```
